# Optimizing a Trainium2 kernel written in Bass

```python
import numpy as np
import jax
import jax.numpy as jnp

def _softmax(x, axis=-1):
    return jax.nn.softmax(x, axis=axis)

def _gelu(x):
    return jax.nn.gelu(x, approximate=True)

def _silu(x):
    return jax.nn.silu(x)

def _sigmoid(x):
    return jax.nn.sigmoid(x)

def _layernorm(x, axis=-1, eps=1e-05):
    m = jnp.mean(x, axis=axis, keepdims=True)
    v = jnp.var(x, axis=axis, keepdims=True)
    return (x - m) / jnp.sqrt(v + eps)

def _scatter_add(tgt, idx, src, axis=0):
    return tgt.at[idx].add(src)

def _segment_sum(src, seg, n):
    return jax.ops.segment_sum(src, seg, n)
kernel_name = 'mk_gnn_preln_d4_gnn_r8_3beef2'

def setup_inputs(seed: int=0):
    np.random.seed(seed)
    _w = jnp.asarray

    def _rec_inputs():
        import jax
        import jax.numpy as jnp
        _gk = jax.random.key(seed)
        x = -0.0005121 + 1.001 * jax.random.normal(jax.random.fold_in(_gk, 1), (6250, 64), jnp.float32)
        src = jax.random.randint(jax.random.fold_in(_gk, 2), (200000,), 0, 6250, jnp.int32)
        dst = jax.random.randint(jax.random.fold_in(_gk, 3), (200000,), 0, 6250, jnp.int32)
        _o = jnp.argsort(dst, stable=True)
        src = src[_o]
        dst = dst[_o]
        edge_attr_16 = 0.000254156 + 0.999948 * jax.random.normal(jax.random.fold_in(_gk, 11), (200000, 16), jnp.float32)
        edge_attr_64 = -6.74381e-05 + 0.999835 * jax.random.normal(jax.random.fold_in(_gk, 12), (200000, 64), jnp.float32)
        return (x, src, dst, edge_attr_16, edge_attr_64)
    x, src, dst, edge_attr_16, edge_attr_64 = _rec_inputs()

    def _L0_gnn_setup():
        import jax, jax.numpy as jnp
        import numpy as np
        N, E = (6250, 100000)
        NODE_DIM, EDGE_DIM, HEADS = (64, 16, 4)
        C = NODE_DIM // HEADS
        NEG_SLOPE = 0.2
        BN_EPS = 1e-05
        key = jax.random.key(seed)
        ks = jax.random.split(key, 12)
        glorot = lambda k, shape: jax.random.normal(k, shape, jnp.float32) * np.sqrt(2.0 / (shape[0] + shape[-1]))
        return {'x': jax.random.normal(ks[0], (N, NODE_DIM), jnp.float32), 'edge_index': jax.random.randint(ks[1], (2, E), 0, N, jnp.int32), 'edge_attr': jax.random.normal(ks[2], (E, EDGE_DIM), jnp.float32), 'W_l': glorot(ks[3], (NODE_DIM, HEADS * C)), 'b_l': jnp.zeros((HEADS * C,), jnp.float32), 'W_r': glorot(ks[4], (NODE_DIM, HEADS * C)), 'b_r': jnp.zeros((HEADS * C,), jnp.float32), 'W_e': glorot(ks[5], (EDGE_DIM, HEADS * C)), 'att': glorot(ks[6], (HEADS, C)), 'bias': jnp.zeros((HEADS * C,), jnp.float32), 'gamma': jnp.ones((NODE_DIM,), jnp.float32), 'beta': jnp.zeros((NODE_DIM,), jnp.float32)}
    _L0_gnn_all = _L0_gnn_setup()
    _L0_gnn_in = {k: v for k, v in _L0_gnn_all.items() if k in ('W_l', 'b_l', 'W_r', 'b_r', 'W_e', 'att', 'bias', 'gamma', 'beta')}
    del _L0_gnn_all

    def _L1_gnn_setup():
        import jax, jax.numpy as jnp
        import numpy as np
        N_NODES = 12500
        N_EDGES = 200000
        IN_DIM = 64
        OUT_DIM = 64
        T_STEPS = 4
        W_SCALE = 0.01
        key = jax.random.key(seed)
        k0, k1, k2, k3, k4, k5 = jax.random.split(key, 6)
        Xv = jax.random.normal(k0, (N_NODES, IN_DIM), dtype=jnp.float32)
        edge_index = jax.random.randint(k1, (2, N_EDGES), 0, N_NODES, dtype=jnp.int64)
        W1 = jax.random.normal(k2, (OUT_DIM, IN_DIM), dtype=jnp.float32) * W_SCALE
        W2 = jax.random.normal(k3, (OUT_DIM, OUT_DIM), dtype=jnp.float32) * W_SCALE
        W3 = jax.random.normal(k4, (OUT_DIM, OUT_DIM), dtype=jnp.float32) * W_SCALE
        W4 = jax.random.normal(k5, (OUT_DIM, 1), dtype=jnp.float32) * W_SCALE
        return {'Xv': Xv, 'edge_index': edge_index, 'W1': W1, 'W2': W2, 'W3': W3, 'W4': W4}
    _L1_gnn_all = _L1_gnn_setup()
    _L1_gnn_in = {k: v for k, v in _L1_gnn_all.items() if k in ('W1', 'W2', 'W3', 'W4')}
    del _L1_gnn_all

    def _L2_gnn_setup():
        import jax, jax.numpy as jnp
        import numpy as np
        N_NODES = 6250
        N_EDGES = 156250
        D_NODE = 64
        D_EDGE = 64
        M_OUT = 64
        U_OUT = 64
        key = jax.random.key(seed)
        k1, k2, k3, k4, k5, k6 = jax.random.split(key, 6)
        H = jax.random.normal(k1, (N_NODES, D_NODE), dtype=jnp.float32)
        Xe = jax.random.normal(k2, (N_EDGES, D_EDGE), dtype=jnp.float32)
        id_Xe = jax.random.randint(k3, (2, N_EDGES), 0, N_NODES, dtype=jnp.int64)
        M_W = jax.random.normal(k4, (M_OUT, D_NODE + D_EDGE), dtype=jnp.float32) * 0.05
        M_b = jnp.zeros((M_OUT,), dtype=jnp.float32)
        U_W = jax.random.normal(k5, (U_OUT, D_NODE + M_OUT), dtype=jnp.float32) * 0.05
        U_b = jnp.zeros((U_OUT,), dtype=jnp.float32)
        return {'H': H, 'Xe': Xe, 'id_Xe': id_Xe, 'M_W': M_W, 'M_b': M_b, 'U_W': U_W, 'U_b': U_b}
    _L2_gnn_all = _L2_gnn_setup()
    _L2_gnn_in = {k: v for k, v in _L2_gnn_all.items() if k in ('M_W', 'M_b', 'U_W', 'U_b')}
    del _L2_gnn_all

    def _L3_gnn_setup():
        import jax, jax.numpy as jnp
        import numpy as np
        N_NODES = 12500
        N_EDGES = 200000
        D_IN = 64
        D_OUT = 64
        K_HOPS = 2
        key = jax.random.key(seed)
        k1, k2, k3, k4 = jax.random.split(key, 4)
        x = jax.random.normal(k1, (N_NODES, D_IN), dtype=jnp.float32)
        W = jax.random.normal(k2, (D_OUT, D_IN), dtype=jnp.float32) * (1.0 / np.sqrt(D_IN))
        b = jax.random.normal(k3, (D_OUT,), dtype=jnp.float32) * 0.01
        edge_index = jax.random.randint(k4, (2, N_EDGES), 0, N_NODES, dtype=jnp.int64)
        return {'x': x, 'W': W, 'b': b, 'edge_index': edge_index}
    _L3_gnn_all = _L3_gnn_setup()
    _L3_gnn_in = {k: v for k, v in _L3_gnn_all.items() if k in ('W', 'b')}
    del _L3_gnn_all
    return {'x': x, 'src': src, 'dst': dst, 'edge_attr_16': edge_attr_16, 'edge_attr_64': edge_attr_64, 'L0_gnn_W_l': _L0_gnn_in['W_l'], 'L0_gnn_b_l': _L0_gnn_in['b_l'], 'L0_gnn_W_r': _L0_gnn_in['W_r'], 'L0_gnn_b_r': _L0_gnn_in['b_r'], 'L0_gnn_W_e': _L0_gnn_in['W_e'], 'L0_gnn_att': _L0_gnn_in['att'], 'L0_gnn_bias': _L0_gnn_in['bias'], 'L0_gnn_gamma': _L0_gnn_in['gamma'], 'L0_gnn_beta': _L0_gnn_in['beta'], 'L1_gnn_W1': _L1_gnn_in['W1'], 'L1_gnn_W2': _L1_gnn_in['W2'], 'L1_gnn_W3': _L1_gnn_in['W3'], 'L1_gnn_W4': _L1_gnn_in['W4'], 'L2_gnn_M_W': _L2_gnn_in['M_W'], 'L2_gnn_M_b': _L2_gnn_in['M_b'], 'L2_gnn_U_W': _L2_gnn_in['U_W'], 'L2_gnn_U_b': _L2_gnn_in['U_b'], 'L3_gnn_W': _L3_gnn_in['W'], 'L3_gnn_b': _L3_gnn_in['b']}

def reference(x, src, dst, edge_attr_16, edge_attr_64, L0_gnn_W_l, L0_gnn_b_l, L0_gnn_W_r, L0_gnn_b_r, L0_gnn_W_e, L0_gnn_att, L0_gnn_bias, L0_gnn_gamma, L0_gnn_beta, L1_gnn_W1, L1_gnn_W2, L1_gnn_W3, L1_gnn_W4, L2_gnn_M_W, L2_gnn_M_b, L2_gnn_U_W, L2_gnn_U_b, L3_gnn_W, L3_gnn_b):
    import jax
    import jax.numpy as jnp

    def _L0_gnn_ref(x, edge_index, edge_attr, W_l, b_l, W_r, b_r, W_e, att, bias, gamma, beta):
        import jax, jax.numpy as jnp
        import numpy as np
        N, E = (6250, 100000)
        NODE_DIM, EDGE_DIM, HEADS = (64, 16, 4)
        C = NODE_DIM // HEADS
        NEG_SLOPE = 0.2
        BN_EPS = 1e-05
        src, dst = (edge_index[0], edge_index[1])
        n = x.shape[0]
        xl = (x @ W_l + b_l).reshape(n, HEADS, C)
        xr = (x @ W_r + b_r).reshape(n, HEADS, C)
        e = (edge_attr @ W_e).reshape(-1, HEADS, C)
        g = jax.nn.leaky_relu(xl[src] + xr[dst] + e, NEG_SLOPE)
        logits = jnp.einsum('ehc,hc->eh', g, att)
        amax = jax.ops.segment_max(logits, dst, num_segments=n)
        ex = jnp.exp(logits - amax[dst])
        denom = jax.ops.segment_sum(ex, dst, num_segments=n)
        alpha = ex / (denom[dst] + 1e-16)
        msg = xl[src] * alpha[..., None]
        out = jax.ops.segment_sum(msg, dst, num_segments=n).reshape(n, HEADS * C) + bias
        mean = out.mean(axis=0)
        var = out.var(axis=0)
        out = (out - mean) * jax.lax.rsqrt(var + BN_EPS) * gamma + beta
        return jax.nn.gelu(out + x, approximate=False)

    def _L1_gnn_ref(Xv, edge_index, W1, W2, W3, W4):
        import jax, jax.numpy as jnp
        import numpy as np
        N_NODES = 12500
        N_EDGES = 200000
        IN_DIM = 64
        OUT_DIM = 64
        T_STEPS = 4
        W_SCALE = 0.01
        n = Xv.shape[0]
        row = edge_index[0]
        col = edge_index[1]
        deg = jax.ops.segment_sum(jnp.ones(row.shape, Xv.dtype), row, num_segments=n)
        w4 = W4[:, 0]
        v3 = deg[:, None] * jax.nn.relu(w4)[None, :] @ W3.T
        base = Xv @ W1.T + v3
        emb = jnp.zeros((n, W1.shape[0]), Xv.dtype)
        for _ in range(T_STEPS):
            neigh = jax.ops.segment_sum(emb[col], row, num_segments=n)
            emb = jax.nn.relu(base + neigh @ W2.T)
        return emb

    def _L2_gnn_ref(H, Xe, id_Xe, M_W, M_b, U_W, U_b):
        import jax, jax.numpy as jnp
        import numpy as np
        N_NODES = 6250
        N_EDGES = 156250
        D_NODE = 64
        D_EDGE = 64
        M_OUT = 64
        U_OUT = 64
        features = H[id_Xe[0]]
        M_in = jnp.concatenate([features, Xe], axis=1)
        Y = jax.nn.relu(M_in @ M_W.T + M_b)
        Z = jax.ops.segment_sum(Y, id_Xe[1], num_segments=H.shape[0])
        U_in = jnp.concatenate([H, Z], axis=1)
        H_next = jax.nn.relu(U_in @ U_W.T + U_b)
        return H_next

    def _L3_gnn_ref(x, W, b, edge_index):
        import jax, jax.numpy as jnp
        import numpy as np
        N_NODES = 12500
        N_EDGES = 200000
        D_IN = 64
        D_OUT = 64
        K_HOPS = 2
        n = x.shape[0]
        self_loops = jnp.arange(n, dtype=edge_index.dtype)
        row = jnp.concatenate([edge_index[0], self_loops])
        col = jnp.concatenate([edge_index[1], self_loops])
        ones = jnp.ones(row.shape[0], dtype=x.dtype)
        deg = jax.ops.segment_sum(ones, col, num_segments=n)
        deg_inv_sqrt = jnp.where(deg > 0, jax.lax.rsqrt(deg), 0.0).astype(x.dtype)
        norm = deg_inv_sqrt[row] * deg_inv_sqrt[col]
        h = x
        for _ in range(K_HOPS):
            h = jax.ops.segment_sum(norm[:, None] * h[row], col, num_segments=n)
        out = h @ W.T + b
        return jax.nn.relu(out)
    edge_index = jnp.stack([src, dst])
    h = jnp.maximum(_layernorm(x, axis=-1), 0.0)
    x = x + _L0_gnn_ref(h, edge_index, edge_attr_16, L0_gnn_W_l, L0_gnn_b_l, L0_gnn_W_r, L0_gnn_b_r, L0_gnn_W_e, L0_gnn_att, L0_gnn_bias, L0_gnn_gamma, L0_gnn_beta)
    h = jnp.maximum(_layernorm(x, axis=-1), 0.0)
    x = x + _L1_gnn_ref(h, edge_index, L1_gnn_W1, L1_gnn_W2, L1_gnn_W3, L1_gnn_W4)
    h = jnp.maximum(_layernorm(x, axis=-1), 0.0)
    x = x + _L2_gnn_ref(h, edge_attr_64, edge_index, L2_gnn_M_W, L2_gnn_M_b, L2_gnn_U_W, L2_gnn_U_b)
    h = jnp.maximum(_layernorm(x, axis=-1), 0.0)
    x = x + _L3_gnn_ref(h, L3_gnn_W, L3_gnn_b, edge_index)
    return x

_drawn_inputs = setup_inputs


def setup_inputs(seed=0):
    import zlib

    import numpy as np

    out = dict(_drawn_inputs(seed))
    spreads = {'L0_gnn_b_l': (0.0, 0.8),
     'L0_gnn_b_r': (0.0, 0.8),
     'L0_gnn_bias': (0.0, 2.0),
     'L0_gnn_gamma': (1.0, 0.2),
     'L0_gnn_beta': (0.0, 0.1),
     'L2_gnn_M_b': (0.0, 0.1),
     'L2_gnn_U_b': (0.0, 0.287)}
    factors = {'L1_gnn_W4': 3.681, 'L3_gnn_b': 31.124}
    for name, (base, spread) in spreads.items():
        noise = np.random.default_rng([zlib.crc32(name.encode()), seed]).standard_normal(out[name].shape)
        drawn = base * np.exp(spread * noise) if base else spread * noise
        out[name] = jnp.asarray(drawn.astype(out[name].dtype))
    for name, factor in factors.items():
        out[name] = (out[name] * factor).astype(out[name].dtype)
    return out
```

```python
from contextlib import ExitStack

import concourse.bass as bass
from concourse import mybir

F32 = mybir.dt.float32
BF16 = mybir.dt.bfloat16
I32 = mybir.dt.int32
ALU = mybir.AluOpType
ACT = mybir.ActivationFunctionType
AX_X = mybir.AxisListType.X

P = 128
D = 64
N = 6250
NT = (N + P - 1) // P
NP = NT * P
E = 200000
HEADS, C = 4, 16
G = 8
BLK = 32
NCH = 1568
EP = NCH * P
NG = NCH // G
QC = NCH // BLK
RUN = QC * P
PAD = NP - 1

WIN = 8
HI = P // WIN
LO = NP // HI
NW = NP // WIN
ITEMS = NCH + NW - 1
IT = (ITEMS + P - 1) // P
IG = 8
IGROUPS = (ITEMS + IG - 1) // IG
BIG = 3.0e38
BN_EPS = 1e-5
OUTSIDE = 1.0e6


class Names:
    pass


class InOrder:

    def __init__(self, eng, sem, base=0):
        self.eng, self.sem, self.base, self.n = eng, sem, base, 0

    def __call__(self, ins):
        self.n += 1
        ins.then_inc(self.sem, 1)
        self.eng.wait_ge(self.sem, self.base + self.n)


def repeat(eng, n, turn):
    turn(0)
    with eng.Fori(1, n) as i:
        turn(i)


def wait_reuse(eng, sem, value):
    if not (isinstance(value, int) and value == 0):
        eng.wait_ge(sem, value)


class Stage:

    def __init__(self, nc, name):
        self.nc, self.name, self.ctx, self.sems = nc, name, ExitStack(), []

    def __enter__(self):
        return self

    def __exit__(self, *a):
        if self.sems and a[0] is None:
            with self.nc.Block() as block:

                @block.gpsimd
                def _(pool):
                    for s in self.sems:
                        pool.sem_clear(s)
        return self.ctx.__exit__(*a)

    def sb(self, name, shape, dt=F32):
        return self.ctx.enter_context(self.nc.sbuf_tensor(f"{self.name}_{name}", shape, dt))

    def ps(self, name, shape, dt=F32):
        return self.ctx.enter_context(self.nc.psum_tensor(f"{self.name}_{name}", shape, dt))

    def sem(self, name):
        self.sems.append(self.ctx.enter_context(self.nc.semaphore(f"{self.name}_{name}")))
        return self.sems[-1]

    def gather_sem(self, g, name):
        return g.top.ctx.enter_context(self.nc.semaphore(f"{self.name}_{name}"))

    def block(self):
        return self.nc.Block()


def spread(ap, shape):
    return ap.to_broadcast(shape)


def constants(nc, g, top):
    g.ident = top.sb("ident", [P, P])
    g.ones = top.sb("ones", [P, P])
    g.count = top.sb("count", [P, P])
    g.dcol = top.sb("dcol", [P, NT])
    g.valid = top.sb("valid", [P, NT])
    g.x = top.sb("x", [P, NT, D])
    g.h = top.sb("h", [P, NT, D])
    with Stage(nc, "const") as st:
        icount = st.sb("icount", [P, P], I32)
        idcol = st.sb("idcol", [P, NT], I32)
        s_pool, s_dve, s_x = st.sem("pool"), st.sem("dve"), st.sem("x")
        with st.block() as block:

            @block.gpsimd
            def _(pool):
                step = InOrder(pool, s_pool)
                step(pool.memset(g.ident[:, :], 0.0))
                step(pool.affine_select(out=g.ident[:, :], in_=g.ident[:, :], compare_op=ALU.not_equal, fill=1.0,
                                        base=0, pattern=[[-1, P]], channel_multiplier=1))
                step(pool.memset(g.ones[:, :], 1.0))
                step(pool.iota(icount[:, :], [[1, P]], base=0, channel_multiplier=0))
                step(pool.iota(idcol[:, :], [[P, NT]], base=0, channel_multiplier=1))

            @block.vector
            def _(dve):
                step = InOrder(dve, s_dve)
                dve.wait_ge(s_pool, 5)
                step(nc.vector.tensor_copy(g.count[:, :], icount[:, :]))
                step(nc.vector.tensor_copy(g.dcol[:, :], idcol[:, :]))
                step(nc.vector.tensor_scalar(g.valid[:, :], g.dcol[:, :], float(N), None, ALU.is_lt))

            @block.sync
            def _(sp):
                sp.dma_start(g.x[:, :, :], g.d["x"].rearrange("(t p) d -> p t d", p=P)).then_inc(s_x, 16)
                sp.wait_ge(s_x, 16)


def layernorm_relu(nc, g, st, block, s_dve, s_act, s_done):
    sq = st.sb("ln_sq", [P, NT, D])
    m = st.sb("ln_m", [P, NT])
    v = st.sb("ln_v", [P, NT])
    full = [P, NT, D]

    @block.vector
    def _(dve):
        step = InOrder(dve, s_dve)
        step(nc.vector.tensor_reduce(m[:, :], g.x[:, :, :], AX_X, ALU.add))
        step(nc.vector.tensor_scalar(m[:, :], m[:, :], 1.0 / D, None, ALU.mult))
        step(nc.vector.tensor_tensor(g.h[:, :, :], g.x[:, :, :], spread(m[:, :].unsqueeze(2), full), ALU.subtract))
        step(nc.vector.tensor_tensor(sq[:, :, :], g.h[:, :, :], g.h[:, :, :], ALU.mult))
        step(nc.vector.tensor_reduce(v[:, :], sq[:, :, :], AX_X, ALU.add))
        step(nc.vector.tensor_scalar(v[:, :], v[:, :], 1.0 / D, 1e-5, ALU.mult, ALU.add))
        dve.wait_ge(s_act, 1)
        step(nc.vector.reciprocal(v[:, :], v[:, :]))
        step(nc.vector.tensor_tensor(g.h[:, :, :], g.h[:, :, :], spread(v[:, :].unsqueeze(2), full), ALU.mult))
        nc.vector.tensor_scalar(g.h[:, :, :], g.h[:, :, :], 0.0, None, ALU.max).then_inc(s_done, 1)

    @block.scalar
    def _(act):
        act.wait_ge(s_dve, 6)
        nc.scalar.activation(v[:, :], v[:, :], ACT.Sqrt).then_inc(s_act, 1)


def node_table(nc, g, name, src, w, width, bias_row, outs, norm=True):
    with Stage(nc, name) as st:
        hT = st.sb("hT", [D + 1, NP])
        ws = st.sb("ws", [D + 1, width])
        res = st.sb("res", [P, NT, width])
        pt = [st.ps(f"pt{k}", [P, 512]) for k in range(2)]
        pw = [st.ps(f"pw{k}", [P, 512]) for k in range(2)]
        s_ln, s_act, s_h = st.sem("ln"), st.sem("act"), st.sem("h")
        s_w, s_one, s_t, s_tc, s_m, s_mc, s_o = (st.sem(k) for k in ("w", "one", "t", "tc", "m", "mc", "o"))
        if norm:
            with st.block() as block:
                layernorm_relu(nc, g, st, block, s_ln, s_act, s_h)
        PT = 4
        PW = 512 // width
        tg = [range(a, min(a + PT, NT)) for a in range(0, NT, PT)]
        wg = [range(a, min(a + PW, NT)) for a in range(0, NT, PW)]
        with st.block() as block:

            @block.gpsimd
            def _(pool):
                nc.gpsimd.memset(hT[D:D + 1, :], 1.0).then_inc(s_one, 1)

            @block.sync
            def _(sp):
                sp.dma_start(ws[0:D, :], w).then_inc(s_w, 16)
                if bias_row is not None:
                    sp.dma_start(ws[D:D + 1, :], bias_row).then_inc(s_w, 16)
                sp.wait_ge(s_w, 16 if bias_row is None else 32)
                sp.wait_ge(s_mc, len(wg))
                for k, o in enumerate(outs):
                    sp.dma_start(o.rearrange("(t p) d -> p t d", p=P), res[:, :, k * D:(k + 1) * D]).then_inc(s_o, 16)
                sp.wait_ge(s_o, 16 * len(outs))

            @block.tensor
            def _(pe):
                for n, r in enumerate(tg):
                    if n >= 2:
                        pe.wait_ge(s_tc, n - 1)
                    for k, t in enumerate(r):
                        mm = nc.tensor.transpose(pt[n % 2][0:D, k * P:(k + 1) * P], src[:, t, :], g.ident[:, :])
                    mm.then_inc(s_t, 1)
                K = D if bias_row is None else D + 1
                pe.wait_ge(s_w, 16 if bias_row is None else 32)
                pe.wait_ge(s_one, 1)
                pe.wait_ge(s_tc, len(tg))
                for n, r in enumerate(wg):
                    if n >= 2:
                        pe.wait_ge(s_mc, n - 1)
                    for k, t in enumerate(r):
                        mm = nc.tensor.matmul(pw[n % 2][:, k * width:(k + 1) * width], hT[0:K, t * P:(t + 1) * P],
                                              ws[0:K, :], start=True, stop=True)
                    mm.then_inc(s_m, 1)

            @block.vector
            def _(dve):
                for n, r in enumerate(tg):
                    dve.wait_ge(s_t, n + 1)
                    nc.vector.tensor_copy(hT[0:D, r[0] * P:(r[-1] + 1) * P], pt[n % 2][0:D, 0:len(r) * P])\
                        .then_inc(s_tc, 1)
                for n, r in enumerate(wg):
                    dve.wait_ge(s_m, n + 1)
                    nc.vector.tensor_copy(res[:, r[0]:r[-1] + 1, :],
                                          pw[n % 2][:, 0:len(r) * width].rearrange("p (t w) -> p t w", w=width))\
                        .then_inc(s_mc, 1)


def segment_ends(nc, g, top):
    g.last_row = top.sb("last_row", [P, NT], I32)
    g.carry_row = top.sb("carry_row", [P, NT], I32)
    g.has = top.sb("has", [P, NT])
    g.con = top.sb("con", [P, NT])
    with Stage(nc, "ends") as st:
        last_i = st.sb("last_i", [P, NCH], I32)
        last = st.sb("last", [P, NCH])
        junk = st.sb("junk", [P, NCH])
        W2 = P + 2
        rows = st.sb("rows", [P, NT, W2], I32)
        cmp = st.sb("cmp", [P, NT, W2])
        cl = st.sb("cl", [P, NT])
        cli = st.sb("cli", [P, NT], I32)
        cnt, z, e0, e1, tmp = (st.sb(k, [P, NT]) for k in ("cnt", "z", "e0", "e1", "tmp"))
        s_l, s_d, s_g = st.sem("l"), st.sem("d"), st.gather_sem(g, "rows")
        s_cl = st.sem("cl")
        with st.block() as block:

            @block.sync
            def _(sp):
                sp.dma_start(last_i[:, :], g.d["last"].partition_broadcast(P)).then_inc(s_l, 16)
                sp.wait_ge(s_l, 16)

            @block.vector
            def _(dve):
                step = InOrder(dve, s_d)
                dve.wait_ge(s_l, 16)
                step(nc.vector.tensor_copy(last[:, :], last_i[:, :]))
                for t in range(NT):
                    step(nc.vector.tensor_scalar(junk[:, :], last[:, :], g.dcol[:, t:t + 1], 0.0, ALU.is_le, ALU.add,
                                                 accum_out=cl[:, t:t + 1]))
                step(nc.vector.tensor_copy(cli[:, :], cl[:, :]))
                dve.sem_inc(s_cl, 1)

            @block.gpsimd
            def _(pool):
                pool.wait_ge(s_cl, 1)
                for t in range(NT):
                    nc.gpsimd.indirect_dma_start(out=rows[:, t, :], out_offset=None, in_=g.d["dst_rows"],
                                                 in_offset=bass.IndirectOffsetOnAxis(ap=cli[:, t:t + 1], axis=0))\
                        .then_inc(s_g, 16)
                pool.wait_ge(s_g, 16 * NT)
        with st.block() as block:

            @block.vector
            def _(dve):
                step = InOrder(dve, s_d, NT + 2)
                v = nc.vector
                bc = lambda k: spread(g.dcol[:, :].unsqueeze(2), [P, NT, k])
                step(v.tensor_tensor(cmp[:, :, 0:P], rows[:, :, 2:W2], bc(P), ALU.is_le))
                step(v.tensor_reduce(cnt[:, :], cmp[:, :, 0:P], AX_X, ALU.add))
                step(v.tensor_tensor(cmp[:, :, :], rows[:, :, :], bc(W2), ALU.is_equal))
                step(v.tensor_reduce(g.has[:, :], cmp[:, :, 1:W2], AX_X, ALU.max))
                step(v.tensor_copy(e0[:, :], cmp[:, :, 0]))
                step(v.tensor_copy(e1[:, :], cmp[:, :, 1]))
                step(v.tensor_scalar(z[:, :], cnt[:, :], 0.0, None, ALU.is_equal))
                step(v.tensor_tensor(tmp[:, :], e0[:, :], e1[:, :], ALU.subtract))
                step(v.tensor_tensor(tmp[:, :], tmp[:, :], z[:, :], ALU.mult))
                step(v.tensor_tensor(tmp[:, :], tmp[:, :], e1[:, :], ALU.add))
                step(v.tensor_tensor(g.con[:, :], tmp[:, :], g.has[:, :], ALU.mult))
                step(v.scalar_tensor_tensor(out=tmp[:, :], in0=cl[:, :], scalar=float(P), in1=cnt[:, :],
                                            op0=ALU.mult, op1=ALU.add))
                step(v.tensor_scalar(g.last_row[:, :], tmp[:, :], -1.0, 0.0, ALU.add, ALU.max))
                step(v.tensor_tensor(tmp[:, :], cl[:, :], z[:, :], ALU.subtract))
                step(v.tensor_scalar(g.carry_row[:, :], tmp[:, :], 0.0, None, ALU.max))


def attention_logits(nc, g, L):
    with Stage(nc, "log") as st:
        R = 2
        ixs, ixd = ([st.sb(f"{k}{s}", [P, G], I32) for s in range(R)] for k in ("ixs", "ixd"))
        src = st.sb("src", [P, NCH], I32)
        dst = st.sb("dst", [P, NCH], I32)
        we = st.sb("we", [16, D])
        att = st.sb("att", [P, D])
        ea = [st.sb(f"ea{s}", [16, G * P]) for s in range(R)]
        gl, gr, t1, t2 = ([st.sb(f"{k}{s}", [P, G, D]) for s in range(R)] for k in ("gl", "gr", "t1", "t2"))
        pe_ = [st.ps(f"pe{s}", [P, G, D]) for s in range(R)]
        s_c, s_go = st.sem("c"), st.sem("go")
        s_ix, s_ea, s_mm, s_used, s_sp = ([st.sem(f"{k}{s}") for s in range(R)] for k in
                                          ("ix", "ea", "mm", "used", "sp"))
        s_gl = [st.gather_sem(g, f"gl{s}") for s in range(R)]
        s_gr = [st.gather_sem(g, f"gr{s}") for s in range(R)]
        s_dve = [st.sem(f"dve{s}") for s in range(R)]
        with st.block() as block:

            @block.sync
            def _(sp):
                sp.dma_start(src[:, :], g.d["src_cols"]).then_inc(s_c, 16)
                sp.dma_start(dst[:, :], g.d["dst_cols"]).then_inc(s_c, 16)
                sp.dma_start(we[:, :], g.d["L0_W_e"]).then_inc(s_c, 16)
                sp.dma_start(att[:, :], g.d["L0_att"].partition_broadcast(P)).then_inc(s_c, 16)
                sp.wait_ge(s_c, 64)
        with st.block() as block:

            @block.sync
            def _(sp):
                def turn(i):
                    for s in range(R):
                        wait_reuse(sp, s_mm[s], i)
                        sp.dma_start(ea[s][:, :], g.d["ea16T"][:, bass.ds((i * R + s) * (G * P), G * P)])\
                            .then_inc(s_ea[s], 16)
                    for s in range(R):
                        sp.wait_ge(s_gl[s], i * (16 * G) + 16 * G)
                        sp.dma_start(g.xg[:, bass.ds((i * R + s) * G, G), :], gl[s][:, :, :]).then_inc(s_sp[s], 16)

                repeat(sp, NG // R, turn)
                for s in range(R):
                    sp.wait_ge(s_sp[s], 16 * (NG // R))

            @block.gpsimd
            def _(pool):
                def turn(i):
                    for s in range(R):
                        wait_reuse(pool, s_used[s], i)
                        wait_reuse(pool, s_sp[s], i * 16)
                        nc.gpsimd.tensor_copy(ixs[s][:, :], src[:, bass.ds((i * R + s) * G, G)]).then_inc(s_ix[s], 1)
                        nc.gpsimd.tensor_copy(ixd[s][:, :], dst[:, bass.ds((i * R + s) * G, G)]).then_inc(s_ix[s], 1)
                        pool.wait_ge(s_ix[s], i * 2 + 2)
                        pool.sem_inc(s_go, 1)
                        for j in range(G):
                            nc.gpsimd.indirect_dma_start(
                                out=gl[s][:, j, :], out_offset=None, in_=g.tab_l,
                                in_offset=bass.IndirectOffsetOnAxis(ap=ixs[s][:, j:j + 1], axis=0))\
                                .then_inc(s_gl[s], 16)
                            nc.gpsimd.indirect_dma_start(
                                out=gr[s][:, j, :], out_offset=None, in_=g.tab_r,
                                in_offset=bass.IndirectOffsetOnAxis(ap=ixd[s][:, j:j + 1], axis=0))\
                                .then_inc(s_gr[s], 16)

                repeat(pool, NG // R, turn)

            @block.tensor
            def _(pe):
                def turn(i):
                    for s in range(R):
                        wait_reuse(pe, s_used[s], i)
                        pe.wait_ge(s_ea[s], i * 16 + 16)
                        for j in range(G):
                            mm = nc.tensor.matmul(pe_[s][:, j, :], ea[s][:, j * P:(j + 1) * P], we[:, :],
                                                  start=True, stop=True)
                        mm.then_inc(s_mm[s], 1)

                repeat(pe, NG // R, turn)

            @block.vector
            def _(dve):
                def turn(i):
                    for s in range(R):
                        step = InOrder(dve, s_dve[s], i * 4)
                        dve.wait_ge(s_mm[s], i + 1)
                        dve.wait_ge(s_gl[s], i * (16 * G) + 16 * G)
                        step(nc.vector.tensor_tensor(t1[s][:, :, :], pe_[s][:, :, :], gl[s][:, :, :], ALU.add))
                        dve.wait_ge(s_gr[s], i * (16 * G) + 16 * G)
                        step(nc.vector.tensor_tensor(t2[s][:, :, :], t1[s][:, :, :], gr[s][:, :, :], ALU.add))
                        step(nc.vector.scalar_tensor_tensor(out=t1[s][:, :, :], in0=t2[s][:, :, :], scalar=0.2,
                                                            in1=t2[s][:, :, :], op0=ALU.mult, op1=ALU.max))
                        step(nc.vector.tensor_tensor(t2[s][:, :, :], t1[s][:, :, :],
                                                     spread(att[:, :].unsqueeze(1), [P, G, D]), ALU.mult))
                        nc.vector.tensor_reduce(
                            L[:, :, bass.ds((i * R + s) * G, G)].rearrange("p h g -> p g h"),
                            t2[s][:, :, :].rearrange("p g (h c) -> p g h c", c=C), AX_X, ALU.add)\
                            .then_inc(s_used[s], 1)

                repeat(dve, NG // R, turn)


def softmax_weights(nc, g, L):
    with Stage(nc, "soft") as st:
        T = st.sb("T", [P, RUN])
        M = st.sb("M", [P, RUN])
        F = st.sb("F", [P, RUN])
        Mi, Fi = M[:, :].bitcast(I32), F[:, :].bitcast(I32)
        Lf = L[:, :, :].rearrange("p h c -> p (h c)")
        Li = Lf.bitcast(I32)
        Lv = Lf.rearrange("p (r q) -> p q r", q=QC)
        ends = st.sb("ends", [P, 2])
        one = st.sb("one", [P, 1])
        carry = st.sb("carry", [P, 2])
        small = st.sb("small", [HEADS, 2, BLK])
        chain = st.sb("chain", [HEADS, BLK + 1])
        pt = [st.ps(f"pt{k}", [P, 4, P]) for k in range(2)]
        s_t, s_tc, s_i, s_d, s_s, s_x = (st.sem(k) for k in ("t", "tc", "i", "d", "s", "x"))
        s_mi = st.sem("mi")
        groups = [range(a, min(a + 4, QC)) for a in range(0, QC, 4)]
        n_d = 0
        with st.block() as block:

            @block.tensor
            def _(pe):
                for n, r in enumerate(groups):
                    if n >= 2:
                        pe.wait_ge(s_tc, n - 1)
                    for k, q in enumerate(r):
                        mm = nc.tensor.transpose(pt[n % 2][:, k, :], Lv[:, q, :], g.ident[:, :])
                    mm.then_inc(s_t, 1)

            @block.vector
            def _(dve):
                for n, r in enumerate(groups):
                    dve.wait_ge(s_t, n + 1)
                    nc.vector.tensor_copy(T[:, r[0] * P:(r[-1] + 1) * P],
                                          pt[n % 2][:, 0:len(r), :].rearrange("p k e -> p (k e)")).then_inc(s_tc, 1)

            @block.sync
            def _(sp):
                for h in range(HEADS):
                    rows = slice(h * BLK, (h + 1) * BLK)
                    sp.dma_start(Mi[rows, :], g.d["dst_ext"][0:EP].rearrange("(b f) -> b f", b=BLK)).then_inc(s_i, 16)
                    sp.dma_start(Fi[rows, :], g.d["dst_ext"][1:EP + 1].rearrange("(b f) -> b f", b=BLK))\
                        .then_inc(s_i, 16)
                sp.wait_ge(s_i, 16 * 2 * HEADS)
        for way, back in enumerate((False, True)):
            first, last = (RUN - 1, 0) if back else (0, RUN - 1)
            data, other_i, res = (F, Li, Lf) if back else (T, Fi, F[:, :])
            rev = (lambda a: a[:, ::-1]) if back else (lambda a: a)
            if back:
                with st.block() as block:

                    @block.sync
                    def _(sp):
                        for h in range(HEADS):
                            rows = slice(h * BLK, (h + 1) * BLK)
                            sp.dma_start(Mi[rows, :], g.d["dst_ext"][2:EP + 2].rearrange("(b f) -> b f", b=BLK))\
                                .then_inc(s_i, 16)
                            sp.dma_start(Li[rows, :], g.d["dst_ext"][1:EP + 1].rearrange("(b f) -> b f", b=BLK))\
                                .then_inc(s_i, 16)
                        sp.wait_ge(s_i, 32 * 2 * HEADS)
            with st.block() as block:

                @block.vector
                def _(dve):
                    step = InOrder(dve, s_d, n_d)
                    v = nc.vector
                    step(v.tensor_tensor(one[:, :], Mi[:, first:first + 1], other_i[:, last:last + 1], ALU.not_equal))
                    step(v.tensor_scalar(ends[:, 0:1], one[:, :], -BIG, None, ALU.mult))
                    step(v.tensor_tensor(M[:, :], other_i, Mi, ALU.not_equal))
                    step(v.tensor_scalar(M[:, :], M[:, :], -BIG, None, ALU.mult))
                    step(v.tensor_tensor_scan(rev(res), rev(M[:, :]), rev(data[:, :]), -BIG, ALU.add, ALU.max))
                    step(v.tensor_copy(ends[:, 1:2], res[:, last:last + 1]))
                    dve.sem_inc(s_s, 1)
                    dve.wait_ge(s_x, 80 * way + 16 * 3)
                    step(v.memset(chain[:, :], -BIG))
                    src = small[:, :, ::-1] if back else small[:, :, :]
                    dst = chain[:, 0:BLK][:, ::-1] if back else chain[:, 1:BLK + 1]
                    step(v.tensor_tensor_scan(dst, src[:, 0, :], src[:, 1, :], -BIG, ALU.add, ALU.max))
                    dve.sem_inc(s_s, 1)
                    dve.wait_ge(s_x, 80 * way + 16 * 5)
                    step(v.tensor_tensor_scan(rev(res), rev(M[:, :]), rev(data[:, :]), carry[:, way:way + 1],
                                              ALU.add, ALU.max))

                @block.sync
                def _(sp):
                    x0 = 80 * way
                    sp.wait_ge(s_s, 2 * way + 1)
                    sp.dma_start(g.scr_ends[:, :], ends[:, :]).then_inc(s_x, 16)
                    sp.wait_ge(s_x, x0 + 16)
                    view = g.scr_ends.rearrange("(h b) k -> h k b", h=HEADS)
                    with nc.allow_non_contiguous_dma(reason="a few values"):
                        for k in range(2):
                            sp.dma_start(small[:, k, :], view[:, k, :]).then_inc(s_x, 16)
                        sp.wait_ge(s_x, x0 + 48)
                        sp.wait_ge(s_s, 2 * way + 2)
                        sp.dma_start(g.scr_chain, chain[:, :]).then_inc(s_x, 16)
                        sp.wait_ge(s_x, x0 + 64)
                        off = 1 if back else 0
                        for h in range(HEADS):
                            sp.dma_start(carry[h * BLK:(h + 1) * BLK, way:way + 1],
                                         g.scr_chain[h, off:off + BLK].unsqueeze(1)).then_inc(s_mi, 16)
                        sp.wait_ge(s_mi, 64 * (way + 1))
                        sp.sem_inc(s_x, 16)
            n_d += 9
        with st.block() as block:

            @block.vector
            def _(dve):
                step = InOrder(dve, s_d, n_d)
                step(nc.vector.tensor_tensor(T[:, :], T[:, :], Lf, ALU.subtract))
                for n, r in enumerate(groups):
                    dve.wait_ge(s_t, len(groups) + n + 1)
                    nc.vector.tensor_copy(
                        Lv[:, r[0]:r[-1] + 1, :], pt[n % 2][:, 0:len(r), :]).then_inc(s_tc, 1)

            @block.scalar
            def _(act):
                act.wait_ge(s_d, n_d + 1)
                nc.scalar.activation(T[:, :], T[:, :], ACT.Exp).then_inc(s_s, 1)

            @block.tensor
            def _(pe):
                pe.wait_ge(s_s, 5)
                for n, r in enumerate(groups):
                    if n >= 2:
                        pe.wait_ge(s_tc, len(groups) + n - 1)
                    for k, q in enumerate(r):
                        mm = nc.tensor.transpose(pt[n % 2][:, k, :], T[:, q * P:(q + 1) * P], g.ident[:, :])
                    mm.then_inc(s_t, 1)


def sum_chunks(nc, g, name, W, L=None, wb=None):
    with Stage(nc, name) as st:
        R = 2
        SB = G // 2
        dst_i = st.sb("dst_i", [P, NCH], I32)
        dst = st.sb("dst", [P, NCH])
        dall = [st.sb(f"dall{s}", [P, G, P], I32) for s in range(R)]
        S = [st.sb(f"S{s}", [P, G, P]) for s in range(R)]
        gl = [st.sb(f"gl{s}", [P, G, D]) for s in range(R)]
        msg = [st.sb(f"msg{s}", [P, G, W]) for s in range(R)]
        o = [st.sb(f"o{s}", [P, G, W]) for s in range(R)]
        pm = [st.ps(f"pm{s}", [P, 2, 512]) for s in range(R)]
        s_c, s_k, s_one, s_go = (st.sem(k) for k in ("c", "k", "one", "go"))
        s_da, s_S, s_msg, s_mm, s_ev, s_out = ([st.sem(f"{k}{s}") for s in range(R)] for k in
                                               ("da", "S", "msg", "mm", "ev", "out"))
        s_gl = [st.gather_sem(g, f"gl{s}") if L is None else st.sem(f"gl{s}") for s in range(R)]
        if L is None:
            src = st.sb("src", [P, NCH], I32)
            wbs = st.sb("wbs", [D, D])
            ixs = [st.sb(f"ixs{s}", [P, G], I32) for s in range(R)]
            ea = [st.sb(f"ea{s}", [D, G * P]) for s in range(R)]
            t1 = [st.sb(f"t1{s}", [P, G, D]) for s in range(R)]
            pb = [st.ps(f"pb{s}", [P, G, D]) for s in range(R)]
            s_ea, s_ix, s_mb, s_t1 = ([st.sem(f"{k}{s}") for s in range(R)] for k in ("ea", "ix", "mb", "t1"))
        with st.block() as block:

            @block.sync
            def _(sp):
                sp.dma_start(dst_i[:, :], g.d["dst_cols"]).then_inc(s_c, 16)
                n = 1
                if L is None:
                    sp.dma_start(src[:, :], g.d["src_cols"]).then_inc(s_c, 16)
                    sp.dma_start(wbs[:, :], wb).then_inc(s_c, 16)
                    n = 3
                sp.wait_ge(s_c, 16 * n)
                sp.sem_inc(s_k, 1)

            @block.vector
            def _(dve):
                dve.wait_ge(s_k, 1)
                nc.vector.tensor_copy(dst[:, :], dst_i[:, :]).then_inc(s_one, 1)
                for s in range(R):
                    nc.vector.memset(msg[s][:, :, :], 1.0).then_inc(s_one, 1)
        with st.block() as block:

            @block.sync
            def _(sp):
                def turn(i):
                    for s in range(R):
                        c0 = (i * R + s) * G
                        wait_reuse(sp, s_S[s], i)
                        sp.dma_start(dall[s][:, :, :].rearrange("p g e -> p (g e)"),
                                     g.d["dst"][bass.ds(c0 * P, G * P)].partition_broadcast(P)).then_inc(s_da[s], 16)
                        if L is None:
                            wait_reuse(sp, s_mb[s], i)
                            sp.dma_start(ea[s][:, :], g.d["ea64T"][:, bass.ds(c0 * P, G * P)]).then_inc(s_ea[s], 16)
                        else:
                            wait_reuse(sp, s_msg[s], i)
                            sp.dma_start(gl[s][:, :, :], g.xg[:, bass.ds(c0, G), :]).then_inc(s_gl[s], 16)

                repeat(sp, NG // R, turn)

            @block.vector
            def _(dve):
                def turn(i):
                    for s in range(R):
                        c0 = (i * R + s) * G
                        wait_reuse(dve, s_mm[s], i)
                        dve.wait_ge(s_da[s], i * 16 + 16)
                        nc.vector.tensor_tensor(
                            S[s][:, :, :], dall[s][:, :, :],
                            spread(dst[:, bass.ds(c0, G)].unsqueeze(2), [P, G, P]), ALU.is_equal)\
                            .then_inc(s_S[s], 1)
                        if L is None:
                            dve.wait_ge(s_mb[s], i + 1)
                            dve.wait_ge(s_gl[s], i * (16 * G) + 16 * G)
                            nc.vector.tensor_tensor(t1[s][:, :, :], pb[s][:, :, :], gl[s][:, :, :], ALU.add)\
                                .then_inc(s_t1[s], 1)
                        else:
                            dve.wait_ge(s_gl[s], i * 16 + 16)
                            w = L[:, :, bass.ds(c0, G)].rearrange("p h g -> p g h")
                            nc.vector.tensor_copy(msg[s][:, :, D:D + HEADS], w)
                            nc.vector.tensor_tensor(
                                msg[s][:, :, 0:D].rearrange("p g (h c) -> p g h c", c=C),
                                gl[s][:, :, :].rearrange("p g (h c) -> p g h c", c=C),
                                spread(w.unsqueeze(3), [P, G, HEADS, C]), ALU.mult).then_inc(s_msg[s], 1)

                repeat(dve, NG // R, turn)

            @block.tensor
            def _(pe):
                def edge_part(i, s):
                    wait_reuse(pe, s_t1[s], i)
                    pe.wait_ge(s_ea[s], i * 16 + 16)
                    for j in range(G):
                        mm = nc.tensor.matmul(pb[s][:, j, :], ea[s][:, j * P:(j + 1) * P], wbs[:, :],
                                              start=True, stop=True)
                    mm.then_inc(s_mb[s], 1)

                def turn(i):
                    if L is None:
                        for s in range(R):
                            edge_part(i, s)
                    for s in range(R):
                        wait_reuse(pe, s_ev[s], i)
                        pe.wait_ge(s_S[s], i + 1)
                        pe.wait_ge(s_msg[s], i + 1)
                        for j in range(G):
                            mm = nc.tensor.matmul(pm[s][:, j // SB, (j % SB) * W:(j % SB + 1) * W],
                                                  S[s][:, j, :], msg[s][:, j, :], start=True, stop=True)
                        mm.then_inc(s_mm[s], 1)

                repeat(pe, NG // R, turn)

            @block.scalar
            def _(act):
                def turn(i):
                    for s in range(R):
                        c0 = (i * R + s) * G
                        if L is None:
                            wait_reuse(act, s_mm[s], i)
                            act.wait_ge(s_t1[s], i + 1)
                            nc.scalar.activation(msg[s][:, :, :], t1[s][:, :, :], ACT.Relu).then_inc(s_msg[s], 1)
                    for s in range(R):
                        c0 = (i * R + s) * G
                        wait_reuse(act, s_out[s], i * 16)
                        act.wait_ge(s_mm[s], i + 1)
                        nc.scalar.activation(
                            o[s][:, :, :].rearrange("p (a b) w -> p a (b w)", a=2),
                            pm[s][:, :, 0:SB * W], ACT.Copy).then_inc(s_ev[s], 1)
                        act.wait_ge(s_ev[s], i + 1)
                        act.dma_start(tot_rows(g, c0, W), o[s][:, :, :]).then_inc(s_out[s], 16)

                repeat(act, NG // R, turn)
                for s in range(R):
                    act.wait_ge(s_out[s], 16 * (NG // R))

            if L is None:

                @block.gpsimd
                def _(pool):
                    def turn(i):
                        for s in range(R):
                            wait_reuse(pool, s_t1[s], i)
                            nc.gpsimd.tensor_copy(ixs[s][:, :], src[:, bass.ds((i * R + s) * G, G)])\
                                .then_inc(s_ix[s], 1)
                            pool.wait_ge(s_ix[s], i + 1)
                            pool.sem_inc(s_go, 1)
                            for j in range(G):
                                nc.gpsimd.indirect_dma_start(
                                    out=gl[s][:, j, :], out_offset=None, in_=g.tab_l,
                                    in_offset=bass.IndirectOffsetOnAxis(ap=ixs[s][:, j:j + 1], axis=0))\
                                    .then_inc(s_gl[s], 16)

                    repeat(pool, NG // R, turn)


def tot_rows(g, c0, W):
    t = g.tot69 if W == D + HEADS + 1 else g.tot64
    return t.rearrange("(c p) w -> p c w", p=P)[:, bass.ds(c0, G), :]


def combine_chunks(nc, g, name, W, U):
    tot = g.tot69 if W == D + HEADS + 1 else g.tot64
    carries = g.car69 if W == D + HEADS + 1 else g.car64
    B = 14
    BP = NCH // B
    with Stage(nc, name) as st:
        lrow = st.sb("lrow", [BP, B, W])
        LT = st.sb("LT", [W, NCH])
        m = st.sb("m", [W, NCH])
        mi = st.sb("mi", [W, NCH], I32)
        mp = st.sb("mp", [W, NCH], I32)
        CT = st.sb("CT", [W, NCH])
        crow = st.sb("crow", [BP, B, W])
        zero = st.sb("zero", [1, W])
        V = st.sb("V", [P, NT, W])
        pt = [st.ps(f"pt{k}", [P, 512]) for k in range(2)]
        s_l, s_t, s_tc, s_d, s_o, s_z = (st.sem(k) for k in ("l", "t", "tc", "d", "o", "z"))
        s_g = st.gather_sem(g, "rows")
        s_m = st.sem("m")
        with st.block() as block:

            @block.sync
            def _(sp):
                sp.dma_start(lrow[:, :, :], tot.rearrange("(b p k) w -> k p b w", p=BP, k=P)[P - 1]).then_inc(s_l, 16)
                sp.wait_ge(s_l, 16)
                sp.dma_start(mi[:, :], g.d["last"].partition_broadcast(W)).then_inc(s_m, 16)
                sp.dma_start(mp[:, :], g.d["last_prev"].partition_broadcast(W)).then_inc(s_m, 16)
                sp.wait_ge(s_m, 32)

            @block.tensor
            def _(pe):
                pe.wait_ge(s_l, 16)
                for b in range(B):
                    if b >= 2:
                        pe.wait_ge(s_tc, b - 1)
                    nc.tensor.transpose(pt[b % 2][0:W, 0:BP], lrow[:, b, :], g.ident[0:BP, 0:BP]).then_inc(s_t, 1)

            @block.vector
            def _(dve):
                for b in range(B):
                    dve.wait_ge(s_t, b + 1)
                    nc.vector.tensor_copy(LT[:, b * BP:(b + 1) * BP], pt[b % 2][0:W, 0:BP]).then_inc(s_tc, 1)
                step = InOrder(dve, s_d)
                dve.wait_ge(s_m, 32)
                step(nc.vector.memset(zero[:, :], 0.0))
                step(nc.vector.tensor_tensor(m[:, :], mi[:, :], mp[:, :], ALU.is_equal))
                dve.wait_ge(s_tc, B)
                step(nc.vector.tensor_tensor_scan(CT[:, :], m[:, :], LT[:, :], 0.0, ALU.mult, ALU.add))

            @block.gpsimd
            def _(pool):
                for t in range(NT):
                    nc.gpsimd.indirect_dma_start(out=V[:, t, :], out_offset=None, in_=tot,
                                                 in_offset=bass.IndirectOffsetOnAxis(ap=g.last_row[:, t:t + 1], axis=0))\
                        .then_inc(s_g, 16)
                pool.wait_ge(s_g, 16 * NT)
        with st.block() as block:

            @block.tensor
            def _(pe):
                for b in range(B):
                    if b >= 2:
                        pe.wait_ge(s_tc, B + b - 1)
                    nc.tensor.transpose(pt[b % 2][0:BP, 0:W], CT[:, b * BP:(b + 1) * BP], g.ident[0:W, 0:W])\
                        .then_inc(s_t, 1)

            @block.vector
            def _(dve):
                for b in range(B):
                    dve.wait_ge(s_t, B + b + 1)
                    nc.vector.tensor_copy(crow[:, b, :], pt[b % 2][0:BP, 0:W]).then_inc(s_tc, 1)

            @block.sync
            def _(sp):
                sp.wait_ge(s_tc, 2 * B)
                sp.dma_start(carries[1:NCH + 1, :].rearrange("(b p) w -> p b w", p=BP), crow[:, :, :])\
                    .then_inc(s_o, 16)
                sp.dma_start(carries[0:1, :], zero[:, :]).then_inc(s_o, 16)
                sp.wait_ge(s_o, 32)

            @block.gpsimd
            def _(pool):
                pool.wait_ge(s_o, 32)
                for t in range(NT):
                    nc.gpsimd.indirect_dma_start(out=U[:, t, :], out_offset=None, in_=carries,
                                                 in_offset=bass.IndirectOffsetOnAxis(ap=g.carry_row[:, t:t + 1], axis=0))\
                        .then_inc(s_g, 16)
                pool.wait_ge(s_g, 32 * NT)
        with st.block() as block:

            @block.vector
            def _(dve):
                step = InOrder(dve, s_z)
                full = [P, NT, W]
                step(nc.vector.tensor_tensor(U[:, :, :], U[:, :, :], spread(g.con[:, :].unsqueeze(2), full), ALU.mult))
                step(nc.vector.tensor_tensor(V[:, :, :], V[:, :, :], spread(g.has[:, :].unsqueeze(2), full), ALU.mult))
                step(nc.vector.tensor_tensor(U[:, :, :], U[:, :, :], V[:, :, :], ALU.add))


def attention_update(nc, g, U):
    with Stage(nc, "bn") as st:
        row = [st.sb(k, [P, D]) for k in ("bias", "gamma", "beta")]
        r = st.sb("r", [P, NT, HEADS])
        o = st.sb("o", [P, NT, D])
        sq = st.sb("sq", [P, NT, D])
        part = st.sb("part", [P, D])
        mean = st.sb("mean", [P, D])
        var = st.sb("var", [P, D])
        ps = st.ps("ps", [P, 512])
        s_c, s_d, s_mm, s_a = (st.sem(k) for k in ("c", "d", "mm", "a"))
        full = [P, NT, D]
        vbc = spread(g.valid[:, :].unsqueeze(2), full)
        with st.block() as block:

            @block.sync
            def _(sp):
                for t, a in zip(row, (g.d["L0_bias"], g.d["L0_gamma"], g.d["L0_beta"])):
                    sp.dma_start(t[:, :], a.partition_broadcast(P)).then_inc(s_c, 16)
                sp.wait_ge(s_c, 48)

            @block.vector
            def _(dve):
                v = nc.vector
                step = InOrder(dve, s_d)
                node = lambda a: spread(a.unsqueeze(1), full)
                head = [P, NT, HEADS, C]
                split = lambda a: a.rearrange("p t (h c) -> p t h c", c=C)
                v.tensor_copy(g.deg_dst[:, :], U[:, :, D + HEADS])
                step(v.tensor_scalar(r[:, :, :], U[:, :, D:D + HEADS], 1e-16, None, ALU.add))
                step(v.reciprocal(r[:, :, :], r[:, :, :]))
                step(v.tensor_tensor(split(o[:, :, :]), split(U[:, :, 0:D]), spread(r[:, :, :].unsqueeze(3), head),
                                     ALU.mult))
                dve.wait_ge(s_c, 48)
                step(v.tensor_tensor(o[:, :, :], o[:, :, :], node(row[0][:, :]), ALU.add))
                step(v.tensor_tensor(sq[:, :, :], o[:, :, :], vbc, ALU.mult))
                step(v.tensor_reduce(part[:, :], sq[:, :, :].rearrange("p t d -> p d t"), AX_X, ALU.add))
                dve.wait_ge(s_mm, 1)
                step(v.tensor_scalar(mean[:, :], ps[:, 0:D], 1.0 / N, None, ALU.mult))
                step(v.tensor_tensor(o[:, :, :], o[:, :, :], node(mean[:, :]), ALU.subtract))
                step(v.tensor_tensor(sq[:, :, :], o[:, :, :], vbc, ALU.mult))
                step(v.tensor_tensor(sq[:, :, :], sq[:, :, :], sq[:, :, :], ALU.mult))
                step(v.tensor_reduce(part[:, :], sq[:, :, :].rearrange("p t d -> p d t"), AX_X, ALU.add))
                dve.wait_ge(s_mm, 2)
                step(v.tensor_scalar(var[:, :], ps[:, D:2 * D], 1.0 / N, BN_EPS, ALU.mult, ALU.add))
                dve.wait_ge(s_a, 1)
                step(v.reciprocal(var[:, :], var[:, :]))
                step(v.tensor_tensor(var[:, :], var[:, :], row[1][:, :], ALU.mult))
                step(v.tensor_tensor(o[:, :, :], o[:, :, :], node(var[:, :]), ALU.mult))
                step(v.tensor_tensor(o[:, :, :], o[:, :, :], node(row[2][:, :]), ALU.add))
                step(v.tensor_tensor(o[:, :, :], o[:, :, :], g.h[:, :, :], ALU.add))
                dve.wait_ge(s_a, 2)
                step(v.tensor_tensor(g.x[:, :, :], g.x[:, :, :], sq[:, :, :], ALU.add))

            @block.tensor
            def _(pe):
                pe.wait_ge(s_d, 6)
                nc.tensor.matmul(ps[:, 0:D], g.ones[:, :], part[:, :], start=True, stop=True).then_inc(s_mm, 1)
                pe.wait_ge(s_d, 11)
                nc.tensor.matmul(ps[:, D:2 * D], g.ones[:, :], part[:, :], start=True, stop=True).then_inc(s_mm, 1)

            @block.scalar
            def _(act):
                act.wait_ge(s_d, 12)
                nc.scalar.activation(var[:, :], var[:, :], ACT.Sqrt).then_inc(s_a, 1)
                act.wait_ge(s_d, 17)
                nc.scalar.activation(sq[:, :, :], o[:, :, :], ACT.Gelu).then_inc(s_a, 1)


def item_columns(nc, g, st0):
    g.rk = st0.sb("rk", [P, IT * P])
    g.lo = st0.sb("lo", [P, IT * P])
    g.keep = st0.sb("keep", [P, IT * P])
    g.flush = st0.sb("flush", [1, IT * P], I32)
    with Stage(nc, "items") as st:
        last_i = st.sb("last_i", [P, NCH], I32)
        ci = st.sb("ci", [P, NCH], I32)
        key = st.sb("key", [P, NCH])
        junk = st.sb("junk", [P, NCH])
        icol = st.sb("icol", [P, IT], I32)
        item = st.sb("item", [P, IT])
        chunk = st.sb("chunk", [P, IT])
        chunk_i = st.sb("chunk_i", [P, IT], I32)
        win = st.sb("win", [P, IT])
        dr = st.sb("dr", [P, IT, P + 2], I32)
        sr = st.sb("sr", [P, IT, P], I32)
        hi = st.sb("hi", [P, IT, P], I32)
        rkr = st.sb("rkr", [P, IT, P])
        lor = st.sb("lor", [P, IT, P])
        cur, near = (st.sb(k, [P, IT * P]) for k in ("cur", "near"))
        end = st.sb("end", [1, 2])
        pt = [st.ps(f"pt{k}", [P, 4, P]) for k in range(2)]
        s_l, s_d, s_io, s_t, s_tc, s_w, s_b, s_e = (st.sem(k) for k in
                                                    ("l", "d", "io", "t", "tc", "w", "b", "e"))
        s_g = st.gather_sem(g, "rows")
        s_go = st.sem("go")
        with st.block() as block:

            @block.sync
            def _(sp):
                sp.dma_start(last_i[:, :], g.d["last"].partition_broadcast(P)).then_inc(s_l, 16)
                sp.wait_ge(s_l, 16)

            @block.gpsimd
            def _(pool):
                nc.gpsimd.iota(ci[:, :], [[1, NCH]], base=0, channel_multiplier=0).then_inc(s_io, 1)
                nc.gpsimd.iota(icol[:, :], [[P, IT]], base=0, channel_multiplier=1).then_inc(s_io, 1)
                pool.wait_ge(s_go, 1)
                for t in range(IT):
                    at = bass.IndirectOffsetOnAxis(ap=chunk_i[:, t:t + 1], axis=0)
                    nc.gpsimd.indirect_dma_start(out=dr[:, t, :], out_offset=None, in_=g.d["dst_rows"], in_offset=at)\
                        .then_inc(s_g, 16)
                    nc.gpsimd.indirect_dma_start(out=sr[:, t, :], out_offset=None, in_=g.d["src_rows"], in_offset=at)\
                        .then_inc(s_g, 16)
                pool.wait_ge(s_g, 32 * IT)

            @block.vector
            def _(dve):
                v = nc.vector
                step = InOrder(dve, s_d)
                dve.wait_ge(s_l, 16)
                dve.wait_ge(s_io, 2)
                step(v.tensor_scalar(last_i[:, :], last_i[:, :], 3, None, ALU.logical_shift_right))
                step(v.tensor_tensor(key[:, :], last_i[:, :], ci[:, :], ALU.add))
                step(v.tensor_copy(item[:, :], icol[:, :]))
                for t in range(IT):
                    step(v.tensor_scalar(junk[:, :], key[:, :], item[:, t:t + 1], 0.0, ALU.is_lt, ALU.add,
                                         accum_out=chunk[:, t:t + 1]))
                step(v.tensor_copy(chunk_i[:, :], chunk[:, :]))
                step(v.tensor_tensor(win[:, :], item[:, :], chunk[:, :], ALU.subtract))
                step(v.memset(end[:, 0:1], -1.0))
                step(v.memset(end[:, 1:2], OUTSIDE))
                dve.sem_inc(s_go, 1)
        with st.block() as block:

            @block.sync
            def _(sp):
                with nc.allow_non_contiguous_dma(reason="one value per item"):
                    sp.dma_start(g.scr_win[1:IT * P + 1].rearrange("(t p) -> p t", p=P), win[:, :]).then_inc(s_w, 16)
                    sp.dma_start(g.scr_win[0:1].unsqueeze(0), end[:, 0:1]).then_inc(s_w, 16)
                    sp.dma_start(g.scr_win[IT * P + 1:IT * P + 2].unsqueeze(0), end[:, 1:2]).then_inc(s_w, 16)
                sp.wait_ge(s_w, 48)
                sp.dma_start(cur[:, :], g.scr_win[1:IT * P + 1].partition_broadcast(P)).then_inc(s_b, 16)
                sp.dma_start(near[:, :], g.scr_win[0:IT * P].partition_broadcast(P)).then_inc(s_b, 16)
                sp.wait_ge(s_b, 32)
                sp.wait_ge(s_e, 1)
                sp.dma_start(near[:, :], g.scr_win[2:IT * P + 2].partition_broadcast(P)).then_inc(s_b, 16)
                sp.wait_ge(s_b, 48)

            @block.vector
            def _(dve):
                v = nc.vector
                step = InOrder(dve, s_d, IT + 7)
                step(v.tensor_scalar(hi[:, :, :], sr[:, :, :], HI - 1, None, ALU.bitwise_and))
                step(v.tensor_scalar(sr[:, :, :], sr[:, :, :], 4, None, ALU.logical_shift_right))
                step(v.tensor_copy(lor[:, :, :], sr[:, :, :]))
                step(v.scalar_tensor_tensor(out=rkr[:, :, :], in0=dr[:, :, 2:P + 2], scalar=float(HI), in1=hi[:, :, :],
                                            op0=ALU.mult, op1=ALU.add))
                step(v.scalar_tensor_tensor(out=rkr[:, :, :], in0=spread(win[:, :].unsqueeze(2), [P, IT, P]),
                                            scalar=-float(P), in1=rkr[:, :, :], op0=ALU.mult, op1=ALU.add))
                for k, (a, to) in enumerate(((rkr, g.rk), (lor, g.lo))):
                    for n, r in enumerate(range(0, IT, 4)):
                        m = min(4, IT - r)
                        dve.wait_ge(s_t, k * 5 + n + 1)
                        v.tensor_copy(to[:, r * P:(r + m) * P],
                                      pt[(k * 5 + n) % 2][:, 0:m, :].rearrange("p k e -> p (k e)")).then_inc(s_tc, 1)
                dve.wait_ge(s_b, 32)
                step(v.tensor_tensor(g.keep[:, :], cur[:, :], near[:, :], ALU.is_equal))
                dve.sem_inc(s_e, 1)
                dve.wait_ge(s_b, 48)
                step(v.tensor_tensor(near[0:1, :], cur[0:1, :], near[0:1, :], ALU.not_equal))
                step(v.tensor_scalar(cur[0:1, :], cur[0:1, :], -float(NW), None, ALU.add))
                step(v.tensor_tensor(cur[0:1, :], cur[0:1, :], near[0:1, :], ALU.mult))
                step(v.tensor_scalar(g.flush[:, :], cur[0:1, :], float(NW), None, ALU.add))

            @block.tensor
            def _(pe):
                for k, a in enumerate((rkr, lor)):
                    pe.wait_ge(s_d, IT + 7 + 5)
                    for n, r in enumerate(range(0, IT, 4)):
                        if k * 5 + n >= 2:
                            pe.wait_ge(s_tc, k * 5 + n - 1)
                        for q in range(min(4, IT - r)):
                            mm = nc.tensor.transpose(pt[(k * 5 + n) % 2][:, q, :], a[:, r + q, :], g.ident[:, :])
                        mm.then_inc(s_t, 1)


def build_counts(nc, g):
    with Stage(nc, "cnt") as st:
        item_columns(nc, g, st)
        c_row = st.sb("c_row", [P, P], BF16)
        c_lo = st.sb("c_lo", [P, LO], mybir.dt.float16)
        c_lo_i = st.sb("c_lo_i", [P, LO], I32)
        ohr = [st.sb(f"ohr{j}", [P, P], BF16) for j in range(IG)]
        ohl = [st.sb(f"ohl{j}", [P, LO], BF16) for j in range(IG)]
        acc = [st.sb(f"acc{j}", [P, LO], BF16) for j in range(IG)]
        pc = [st.ps(f"pc{j}", [P, 512]) for j in range(IG)]
        s_io, s_c = st.sem("io"), st.sem("c")
        s_oh, s_mm, s_acc, s_st = ([st.sem(f"{k}{j}") for j in range(IG)] for k in ("oh", "mm", "acc", "st"))
        with st.block() as block:

            @block.gpsimd
            def _(pool):
                nc.gpsimd.iota(c_lo_i[:, :], [[1, LO]], base=0, channel_multiplier=0).then_inc(s_io, 1)

            @block.vector
            def _(dve):
                dve.wait_ge(s_io, 1)
                nc.vector.tensor_copy(c_lo[:, :], c_lo_i[:, :]).then_inc(s_c, 1)
                nc.vector.tensor_copy(c_row[:, :], g.count[:, :]).then_inc(s_c, 1)
                nc.vector.memset(acc[IG - 1][:, :], 0.0).then_inc(s_c, 1)
        with st.block() as block:

            @block.vector
            def _(dve):
                def turn(i):
                    for j in range(IG):
                        wait_reuse(dve, s_mm[j], i)
                        nc.vector.tensor_scalar(ohr[j][:, :], c_row[:, :], g.rk[:, bass.ds(i * IG + j, 1)], None,
                                                ALU.is_equal).then_inc(s_oh[j], 1)
                        nc.vector.tensor_scalar(ohl[j][:, :], c_lo[:, :], g.lo[:, bass.ds(i * IG + j, 1)], None,
                                                ALU.is_equal).then_inc(s_oh[j], 1)
                    for j in range(IG):
                        wait_reuse(dve, s_st[j], i * 16)
                        dve.wait_ge(s_mm[j], i + 1)
                        wait_reuse(dve, s_acc[j - 1], i if j == 0 else i + 1)
                        nc.vector.scalar_tensor_tensor(
                            out=acc[j][:, :], in0=acc[j - 1][:, :], scalar=g.keep[:, bass.ds(i * IG + j, 1)],
                            in1=pc[j][:, 0:LO], op0=ALU.mult, op1=ALU.add).then_inc(s_acc[j], 1)

                repeat(dve, IGROUPS, turn)

            @block.tensor
            def _(pe):
                def turn(i):
                    for j in range(IG):
                        wait_reuse(pe, s_acc[j], i)
                        pe.wait_ge(s_oh[j], i * 2 + 2)
                        nc.tensor.matmul(pc[j][:, 0:LO], ohr[j][:, :], ohl[j][:, :], start=True, stop=True)\
                            .then_inc(s_mm[j], 1)

                repeat(pe, IGROUPS, turn)

            @block.sync
            def _(sp):
                def turn(i):
                    for j in range(IG):
                        w = sp.value_load(g.flush[0:1, bass.ds(i * IG + j, 1)], min_val=0, max_val=NW)
                        sp.wait_ge(s_acc[j], i + 1)
                        sp.dma_start(g.A[bass.ds(w * P, P), :], acc[j][:, :], cond=(w < NW)).then_inc(s_st[j], 16)

                repeat(sp, IGROUPS, turn)
                for j in range(IG):
                    sp.wait_ge(s_st[j], 16 * IGROUPS)


def transpose_counts(nc, g):
    KB = 4
    gr = [range(a, min(a + KB, NT)) for a in range(0, NT, KB)]
    NK, NB = len(gr), 7
    per = {0: (NK + 1) // 2, 1: NK // 2}
    R = 2
    with Stage(nc, "tr") as st:
        eye = st.sb("eye", [P, P], BF16)
        one = st.sb("one", [P, 1], BF16)
        a = [st.sb(f"a{s}", [P, NP], BF16) for s in range(R)]
        at = [st.sb(f"at{s}", [P, NT, P], BF16) for s in range(R)]
        deg = st.sb("deg", [P, NT])
        pb = [st.ps(f"pb{k}", [P, 512]) for k in range(NB)]
        pd = st.ps("pd", [P, 512])
        s_c, s_pe, s_o, s_z = (st.sem(k) for k in ("c", "pe", "o", "z"))
        s_ev = [st.sem("dve"), st.sem("act")]
        s_in, s_used, s_st = ([st.sem(f"{k}{s}") for s in range(R)] for k in ("in", "used", "st"))
        Arows = g.A[0:NP * HI, :].rearrange("(n h) l -> n (h l)", h=HI)
        with st.block() as block:

            @block.vector
            def _(dve):
                nc.vector.tensor_copy(eye[:, :], g.ident[:, :]).then_inc(s_c, 1)
                nc.vector.memset(one[:, :], 1.0).then_inc(s_c, 1)

        def tiles(eng, body):
            body(R - 1, 0, 0)
            def turn(i):
                for s in range(R):
                    body(s, i if s < R - 1 else i + 1, i * R + (s + 1))

            repeat(eng, NT // R, turn)

        with st.block() as block:

            @block.sync
            def _(sp):
                def body(s, n, dt):
                    wait_reuse(sp, s_used[s], n)
                    sp.dma_start(a[s][:, :], Arows[bass.ds(dt * P, P), :]).then_inc(s_in[s], 16)
                tiles(sp, body)

            @block.tensor
            def _(pe):
                def body(s, n, dt):
                    first = isinstance(dt, int) and dt == 0
                    pe.wait_ge(s_in[s], n * 16 + 16)
                    for k, r in enumerate(gr):
                        if k == 0:
                            wait_reuse(pe, s_ev[0], dt * per[0])
                            wait_reuse(pe, s_ev[1], dt * per[1])
                        elif k >= NB:
                            e = (k - NB) % 2
                            pe.wait_ge(s_ev[e], dt * per[e] + ((k - NB) // 2 + 1))
                        for m, q in enumerate(r):
                            block_ = a[s][:, q * P:(q + 1) * P]
                            nc.tensor.matmul(pd[:, q:q + 1], block_, one[:, :], start=first and q == 0, stop=False,
                                             skip_group_check=True)
                            mm = nc.tensor.matmul(pb[k % NB][:, m * P:(m + 1) * P], block_, eye[:, :],
                                                  start=True, stop=True)
                        mm.then_inc(s_pe, 1)
                    pe.wait_ge(s_pe, dt * NK + NK)
                    pe.sem_inc(s_used[s], 1)
                tiles(pe, body)

            def evacuate(eng, copy, e):
                def body(s, n, dt):
                    wait_reuse(eng, s_st[s], n * 16)
                    for k in range(e, NK, 2):
                        r = gr[k]
                        eng.wait_ge(s_pe, dt * NK + k + 1)
                        copy(at[s][:, r[0]:r[-1] + 1, :], pb[k % NB][:, 0:len(r) * P]
                             .rearrange("p (m e) -> p m e", e=P)).then_inc(s_ev[e], 1)
                    if e:
                        eng.wait_ge(s_ev[0], dt * per[0] + per[0])
                        eng.wait_ge(s_ev[1], dt * per[1] + per[1])
                        eng.dma_start(g.AT[bass.ds(dt * P, P), :], at[s][:, :, :].rearrange("p t e -> p (t e)"))\
                            .then_inc(s_st[s], 16)
                return body

            @block.vector
            def _(dve):
                tiles(dve, evacuate(dve, nc.vector.tensor_copy, 0))

            @block.scalar
            def _(act):
                tiles(act, evacuate(act, lambda o, x: nc.scalar.activation(o, x, ACT.Copy), 1))
                act.wait_ge(s_st[0], 16 * (NT // R))
                act.wait_ge(s_st[1], 16 * (NT // R + 1))
        with st.block() as block:

            @block.vector
            def _(dve):
                nc.vector.tensor_copy(deg[:, :], pd[:, 0:NT]).then_inc(s_c, 1)

            @block.sync
            def _(sp):
                sp.wait_ge(s_c, 3)
                with nc.allow_non_contiguous_dma(reason="one value per node"):
                    sp.dma_start(g.scr_deg.rearrange("(t p) -> p t", p=P), deg[:, :]).then_inc(s_o, 16)
                    sp.wait_ge(s_o, 16)
                    view = g.scr_deg.rearrange("(h t l) -> l h t", h=HI, l=WIN)
                    for k in range(WIN):
                        sp.dma_start(g.deg_src[k * HI:(k + 1) * HI, :], view[k]).then_inc(s_z, 16)
                    sp.wait_ge(s_z, 16 * WIN)


def split3(dve, step, x, parts, r):
    v = dve
    step(v.tensor_copy(parts[0], x))
    step(v.tensor_tensor(r, x, parts[0], ALU.subtract))
    step(v.tensor_copy(parts[1], r))
    step(v.tensor_tensor(r, r, parts[1], ALU.subtract))
    step(v.tensor_copy(parts[2], r))


def layer1(nc, g):
    PASSES = 3
    R = 7
    HB = 8
    with Stage(nc, "l1") as st:
        base = st.sb("base", [P, NT, D])
        with Stage(nc, "l1n") as sn:
            s_ln, s_act, s_h = sn.sem("ln"), sn.sem("act"), sn.sem("h")
            with sn.block() as block:
                layernorm_relu(nc, g, sn, block, s_ln, s_act, s_h)
        node_product(nc, g, "l1b", [g.h], g.d["L1_W1T"], base)
        with Stage(nc, "l1v") as sn:
            w4 = sn.sb("w4", [D, 1])
            w3 = sn.sb("w3", [D, D])
            vrow = sn.sb("vrow", [P, D])
            outer = sn.sb("outer", [P, NT, D])
            pv = sn.ps("pv", [P, 512])
            s_c, s_d, s_m = sn.sem("c"), sn.sem("d"), sn.sem("m")
            full = [P, NT, D]
            with sn.block() as block:

                @block.sync
                def _(sp):
                    with nc.allow_non_contiguous_dma(reason="a column of 64"):
                        sp.dma_start(w4[:, :], g.d["L1_W4"]).then_inc(s_c, 16)
                    sp.dma_start(w3[:, :], g.d["L1_W3T"]).then_inc(s_c, 16)
                    sp.wait_ge(s_c, 32)

                @block.vector
                def _(dve):
                    step = InOrder(dve, s_d)
                    dve.wait_ge(s_c, 32)
                    step(nc.vector.tensor_scalar(w4[:, :], w4[:, :], 0.0, None, ALU.max))
                    dve.wait_ge(s_m, 1)
                    step(nc.vector.tensor_copy(vrow[:, :], pv[:, 0:D]))
                    step(nc.vector.tensor_tensor(outer[:, :, :], spread(vrow[:, :].unsqueeze(1), full),
                                                 spread(g.deg_src[:, :].unsqueeze(2), full), ALU.mult))
                    step(nc.vector.tensor_tensor(base[:, :, :], base[:, :, :], outer[:, :, :], ALU.add))

                @block.tensor
                def _(pe):
                    pe.wait_ge(s_d, 1)
                    nc.tensor.matmul(pv[:, 0:D], spread(w4[:, :], [D, P]), w3[:, :], start=True, stop=True)\
                        .then_inc(s_m, 1)
        E3 = st.sb("E3", [P, NT, 4 * D], BF16)
        r = st.sb("r", [P, NT, D])
        emb = st.sb("emb", [P, NT, D])
        nb = st.sb("nb", [P, NP])
        w2 = st.sb("w2", [P, D])
        a = [st.sb(f"a{s}", [P, NP // 2], BF16) for s in range(R)]
        pn = [st.ps(f"pn{b}", [P, 512]) for b in range(HB)]
        s_c, s_e, s_sw, s_evd, s_eva, s_nm, s_add = (st.sem(k) for k in ("c", "e", "sw", "evd", "eva", "nm", "add"))
        s_in, s_used = ([st.sem(f"{k}{s}") for s in range(R)] for k in ("in", "used"))
        Arows = g.A[0:NP * HI, :].rearrange("(n h) l -> n (h l)", h=HI)
        TB = 7
        parts = [E3[:, :, k * D:(k + 1) * D] for k in range(3)]
        per = 6
        with st.block() as block:

            @block.sync
            def _(sp):
                sp.dma_start(w2[:, :], g.d["L1_W2T2"]).then_inc(s_c, 16)
                sp.wait_ge(s_c, 16)
                for n in range(2 * PASSES):
                    half = n % 2
                    def turn(i):
                        for s in range(R):
                            wait_reuse(sp, s_used[s], i + n * (NT // R))
                            sp.dma_start(a[s][:, :], Arows[bass.ds((i * R + s) * P, P),
                                                           half * (NP // 2):(half + 1) * (NP // 2)])\
                                .then_inc(s_in[s], 16)

                    repeat(sp, NT // R, turn)

            @block.tensor
            def _(pe):
                def tile(n, i, s, first):
                    pe.wait_ge(s_in[s], (i + n * (NT // R)) * 16 + 16)
                    for part in range(2):
                        lhs = E3[:, i * R + s, part * P:(part + 1) * P] if isinstance(i, int) else \
                            E3[:, :, :].rearrange("p t e -> p (t e)")[:, bass.ds((i * R + s) * (4 * D) + part * P, P)]
                        for b in range(HB):
                            mm = nc.tensor.matmul(pn[b][:, 0:LO], lhs, a[s][:, b * LO:(b + 1) * LO],
                                                  start=first and part == 0, stop=False, skip_group_check=True)
                    mm.then_inc(s_used[s], 1)

                pe.wait_ge(s_c, 16)
                for n in range(2 * PASSES):
                    if n % 2 == 0:
                        pe.wait_ge(s_e, per * (n // 2 + 1) + 1)
                    wait_reuse(pe, s_evd, (HB // 2) * n)
                    wait_reuse(pe, s_eva, (HB // 2) * n)
                    for s in range(R):
                        tile(n, 0, s, s == 0)
                    with pe.Fori(1, NT // R) as i:
                        for s in range(R):
                            tile(n, i, s, False)
                    pe.wait_ge(s_used[R - 1], (n + 1) * (NT // R))
                    pe.sem_inc(s_sw, 1)
                    if n % 2:
                        p = n // 2
                        pe.wait_ge(s_evd, (HB // 2) * (n + 1))
                        pe.wait_ge(s_eva, (HB // 2) * (n + 1))
                        for b in range(NT // TB):
                            for m in range(TB):
                                t = b * TB + m
                                mm = nc.tensor.matmul(pn[b][:, m * D:(m + 1) * D], nb[:, t * P:(t + 1) * P], w2[:, :],
                                                      start=True, stop=True)
                            mm.then_inc(s_nm, 1)

            def evacuate(eng, copy, n, banks, sem):
                eng.wait_ge(s_sw, n + 1)
                if n % 2 == 0 and n:
                    eng.wait_ge(s_nm, (NT // TB) * (n // 2))
                for b in banks:
                    hi = (n % 2) * HB + b
                    copy(nb[:, :].rearrange("p (l h) -> p l h", h=HI)[:, :, hi], pn[b][:, 0:LO]).then_inc(sem, 1)

            @block.vector
            def _(dve):
                step = InOrder(dve, s_e)
                step(nc.vector.memset(E3[:, :, 3 * D:4 * D], 0.0))
                step(nc.vector.tensor_scalar(emb[:, :, :], base[:, :, :], 0.0, None, ALU.max))
                for p in range(PASSES):
                    if p:
                        step(nc.vector.tensor_scalar(emb[:, :, :], emb[:, :, :], 0.0, None, ALU.max))
                    split3(nc.vector, step, emb[:, :, :], parts, r[:, :, :])
                    if p == 0:
                        assert step.n == per + 1
                    for n in (2 * p, 2 * p + 1):
                        evacuate(dve, nc.vector.tensor_copy, n, range(0, HB // 2), s_evd)
                    for b in range(NT // TB):
                        dve.wait_ge(s_nm, (NT // TB) * p + b + 1)
                        nc.vector.tensor_tensor(emb[:, b * TB:(b + 1) * TB, :],
                                                pn[b][:, 0:TB * D].rearrange("p (t d) -> p t d", d=D),
                                                base[:, b * TB:(b + 1) * TB, :], ALU.add).then_inc(s_add, 1)
                    dve.wait_ge(s_add, (NT // TB) * (p + 1))
                step(nc.vector.tensor_scalar(emb[:, :, :], emb[:, :, :], 0.0, None, ALU.max))
                step(nc.vector.tensor_tensor(g.x[:, :, :], g.x[:, :, :], emb[:, :, :], ALU.add))

            @block.scalar
            def _(act):
                for n in range(2 * PASSES):
                    evacuate(act, lambda o, x: nc.scalar.activation(o, x, ACT.Copy), n, range(HB // 2, HB), s_eva)


def node_product(nc, g, name, srcs, w, out, post=None):
    K = D * len(srcs)
    with Stage(nc, name) as st:
        ws = st.sb("ws", [K, D])
        sT = st.sb("sT", [K, NP])
        pt = [st.ps(f"pt{k}", [P, 512]) for k in range(2)]
        pw = [st.ps(f"pw{k}", [P, 512]) for k in range(2)]
        s_w, s_t, s_tc, s_m, s_mc, s_j, s_jc = (st.sem(k) for k in ("w", "t", "tc", "m", "mc", "j", "jc"))
        joined = srcs[0]
        if len(srcs) > 1:
            joined = st.sb("joined", [P, NT, K])
            with st.block() as block:

                @block.vector
                def _(dve):
                    for k, s in enumerate(srcs):
                        nc.vector.tensor_copy(joined[:, :, k * D:(k + 1) * D], s[:, :, 0:D]).then_inc(s_j, 1)
        tg = [range(a, min(a + 4, NT)) for a in range(0, NT, 4)]
        wg = [range(a, min(a + 8, NT)) for a in range(0, NT, 8)]
        with st.block() as block:

            @block.sync
            def _(sp):
                sp.dma_start(ws[:, :], w).then_inc(s_w, 16)
                sp.wait_ge(s_w, 16)

            @block.tensor
            def _(pe):
                for n, r in enumerate(tg):
                    if n >= 2:
                        pe.wait_ge(s_tc, n - 1)
                    for k, t in enumerate(r):
                        mm = nc.tensor.transpose(pt[n % 2][0:K, k * P:(k + 1) * P], joined[:, t, :], g.ident[:, :])
                    mm.then_inc(s_t, 1)
                pe.wait_ge(s_w, 16)
                pe.wait_ge(s_tc, len(tg))
                for n, r in enumerate(wg):
                    if n >= 2:
                        pe.wait_ge(s_mc, n - 1)
                    for k, t in enumerate(r):
                        mm = nc.tensor.matmul(pw[n % 2][:, k * D:(k + 1) * D], sT[:, t * P:(t + 1) * P], ws[:, :],
                                              start=True, stop=True)
                    mm.then_inc(s_m, 1)

            @block.vector
            def _(dve):
                for n, r in enumerate(tg):
                    dve.wait_ge(s_t, n + 1)
                    nc.vector.tensor_copy(sT[:, r[0] * P:(r[-1] + 1) * P], pt[n % 2][0:K, 0:len(r) * P])\
                        .then_inc(s_tc, 1)
                for n, r in enumerate(wg):
                    dve.wait_ge(s_m, n + 1)
                    nc.vector.tensor_copy(out[:, r[0]:r[-1] + 1, :],
                                          pw[n % 2][:, 0:len(r) * D].rearrange("p (t w) -> p t w", w=D))\
                        .then_inc(s_mc, 1)


def add_relu(nc, g, name, t, bias):
    with Stage(nc, name) as st:
        row = st.sb("row", [P, D])
        s_c, s_d = st.sem("c"), st.sem("d")
        with st.block() as block:

            @block.sync
            def _(sp):
                sp.dma_start(row[:, :], bias.partition_broadcast(P)).then_inc(s_c, 16)
                sp.wait_ge(s_c, 16)

            @block.vector
            def _(dve):
                step = InOrder(dve, s_d)
                dve.wait_ge(s_c, 16)
                step(nc.vector.tensor_tensor(t[:, :, :], t[:, :, :], spread(row[:, :].unsqueeze(1), [P, NT, D]),
                                             ALU.add))
                step(nc.vector.scalar_tensor_tensor(out=g.x[:, :, :], in0=t[:, :, :], scalar=0.0, in1=g.x[:, :, :],
                                                    op0=ALU.max, op1=ALU.add))


def layer2(nc, g):
    node_table(nc, g, "tab2", g.h, g.d["L2_MhT"], D, g.d["L2_Mb"], [g.tab_l])
    sum_chunks(nc, g, "sum2", D, wb=g.d["L2_MxT"])
    with Stage(nc, "l2") as st:
        Z = st.sb("Z", [P, NT, D])
        combine_chunks(nc, g, "comb2", D, Z)
        node_product(nc, g, "l2u", [g.h, Z], g.d["L2_UT"], Z)
        add_relu(nc, g, "l2r", Z, g.d["L2_Ub"])


def layer3(nc, g):
    R = 2
    with Stage(nc, "l3") as st:
        with Stage(nc, "l3n") as sn:
            s_ln, s_act, s_h = sn.sem("ln"), sn.sem("act"), sn.sem("h")
            with sn.block() as block:
                layernorm_relu(nc, g, sn, block, s_ln, s_act, s_h)
        dis = st.sb("dis", [P, NT])
        y = st.sb("y", [P, NT, D])
        r = st.sb("r", [P, NT, D])
        E3 = st.sb("E3", [P, NT, 3 * D], BF16)
        Eq = st.sb("Eq", [P, NT, 3 * D], BF16)
        at = [st.sb(f"at{s}", [P, NP], BF16) for s in range(R)]
        pn = [st.ps(f"pn{s}", [P, 512]) for s in range(R)]
        s_d, s_a, s_w, s_go = (st.sem(k) for k in ("d", "a", "w", "go"))
        s_q, s_rd = st.sem("q"), st.sem("rd")
        s_in, s_used, s_mm, s_y = ([st.sem(f"{k}{s}") for s in range(R)] for k in ("in", "used", "mm", "y"))
        full = [P, NT, D]
        parts = [E3[:, :, k * D:(k + 1) * D] for k in range(3)]
        with st.block() as block:

            @block.vector
            def _(dve):
                step = InOrder(dve, s_d)
                step(nc.vector.tensor_scalar(dis[:, :], g.deg_dst[:, :], 1.0, None, ALU.add))
                dve.wait_ge(s_a, 1)
                step(nc.vector.reciprocal(dis[:, :], dis[:, :]))

            @block.scalar
            def _(act):
                act.wait_ge(s_d, 1)
                nc.scalar.activation(dis[:, :], dis[:, :], ACT.Sqrt).then_inc(s_a, 1)
        n_d = 2
        for hop in range(2):
            src = g.h if hop == 0 else y
            dbc = spread(dis[:, :].unsqueeze(2), full)
            with st.block() as block:

                @block.vector
                def _(dve):
                    step = InOrder(dve, s_d, n_d)
                    step(nc.vector.tensor_tensor(g.h[:, :, :], src[:, :, :], dbc, ALU.mult))
                    split3(nc.vector, step, g.h[:, :, :], parts, r[:, :, :])

                @block.sync
                def _(sp):
                    sp.wait_ge(s_d, n_d + 6)
                    view = g.scr_e3.rearrange("(h t l) w -> l h t w", h=HI, l=WIN)
                    for k in range(WIN):
                        sp.dma_start(view[k], E3[k * HI:(k + 1) * HI, :, :]).then_inc(s_w, 16)
                    sp.wait_ge(s_w, 16 * WIN * (hop + 1))
                    sp.dma_start(Eq[:, :, :], g.scr_e3.rearrange("(t p) w -> p t w", p=P)).then_inc(s_rd, 16)
                    sp.wait_ge(s_rd, 16 * (hop + 1))
            n_d += 6

            b = [hop * (NT // R + 1), hop * (NT // R)]

            def tiles(eng, body):
                def turn(i):
                    for s in range(R):
                        body(i, s, i * R + s)

                repeat(eng, NT // R, turn)
                body(NT // R, 0, NT - 1)

            with st.block() as block:

                @block.sync
                def _(sp):
                    def body(i, s, dt):
                        wait_reuse(sp, s_mm[s], i + b[s])
                        sp.dma_start(at[s][:, :], g.AT[bass.ds(dt * P, P), :]).then_inc(s_in[s], 16)
                    tiles(sp, body)

                @block.tensor
                def _(pe):
                    def body(i, s, dt):
                        wait_reuse(pe, s_y[s], i + b[s])
                        pe.wait_ge(s_in[s], (i + b[s]) * 16 + 16)
                        for q in range(NT):
                            mm = nc.tensor.matmul(pn[s][:, 0:3 * D], at[s][:, q * P:(q + 1) * P], Eq[:, q, :],
                                                  start=(q == 0), stop=(q == NT - 1))
                        mm.then_inc(s_mm[s], 1)
                    tiles(pe, body)

                @block.vector
                def _(dve):
                    def body(i, s, dt):
                        dve.wait_ge(s_mm[s], i + b[s] + 1)
                        dve.sem_inc(s_go, 1)
                        yv = y[:, :, :].rearrange("p t d -> p (t d)")[:, bass.ds(dt * D, D)]
                        nc.vector.tensor_reduce(yv, pn[s][:, 0:3 * D].rearrange("p (k d) -> p d k", k=3), AX_X,
                                                ALU.add).then_inc(s_y[s], 1)
                    tiles(dve, body)
            with st.block() as block:

                @block.vector
                def _(dve):
                    step = InOrder(dve, s_d, n_d)
                    step(nc.vector.tensor_tensor(y[:, :, :], y[:, :, :], g.h[:, :, :], ALU.add))
                    step(nc.vector.tensor_tensor(y[:, :, :], y[:, :, :], dbc, ALU.mult))
            n_d += 2
        node_product(nc, g, "l3w", [y], g.d["L3_WT"], r)
        add_relu(nc, g, "l3r", r, g.d["L3_b"])


def scratch(nc, g):
    def dram(name, shape, dt=F32):
        return nc.dram_tensor(name, shape, dt).ap()
    g.tab_l, g.tab_r = dram("tab_l", [NP, D]), dram("tab_r", [NP, D])
    g.xg = dram("xg", [P, NCH, D])
    g.tot69, g.tot64 = dram("tot69", [EP, D + HEADS + 1]), dram("tot64", [EP, D])
    g.car69, g.car64 = dram("car69", [NCH + 1, D + HEADS + 1]), dram("car64", [NCH + 1, D])
    g.A = dram("A", [(NW + 1) * P, LO], BF16)
    g.AT = dram("AT", [NP, NP], BF16)
    g.scr_win, g.scr_deg, g.scr_e3 = dram("scr_win", [IT * P + 2]), dram("scr_deg", [NP]), dram("scr_e3", [NP, 3 * D], BF16)
    g.scr_ends, g.scr_chain = dram("scr_ends", [P, 2]), dram("scr_chain", [HEADS, BLK + 1])


def layer0(nc, g):
    with Stage(nc, "l0") as st:
        node_table(nc, g, "tab0", g.h, g.d["L0_Wlr"], 2 * D, g.d["L0_blr"], [g.tab_l, g.tab_r])
        with Stage(nc, "l0e") as se:
            L = se.sb("L", [P, HEADS, NCH])
            attention_logits(nc, g, L)
            softmax_weights(nc, g, L)
            sum_chunks(nc, g, "sum0", D + HEADS + 1, L=L)
        g.U = st.sb("U", [P, NT, D + HEADS + 1])
        combine_chunks(nc, g, "comb0", D + HEADS + 1, g.U)
        attention_update(nc, g, g.U)


def gnn_kernel(nc, d, out, upto=4):
    g = Names()
    g.d = d
    scratch(nc, g)
    with Stage(nc, "top") as top:
        g.top = top
        constants(nc, g, top)
        segment_ends(nc, g, top)
        g.deg_dst = top.sb("deg_dst", [P, NT])
        g.deg_src = top.sb("deg_src", [P, NT])
        layer0(nc, g)
        if upto > 1:
            build_counts(nc, g)
            transpose_counts(nc, g)
            layer1(nc, g)
        if upto > 2:
            layer2(nc, g)
        if upto > 3:
            layer3(nc, g)
        with Stage(nc, "out") as st:
            s_out = st.sem("done")
            with st.block() as block:

                @block.sync
                def _(sp):
                    full = (N // P) * P
                    sp.dma_start(out[0:full, :].rearrange("(t p) d -> p t d", p=P), g.x[:, 0:N // P, :])\
                        .then_inc(s_out, 16)
                    sp.dma_start(out[full:N, :], g.x[0:N - full, N // P, :]).then_inc(s_out, 16)
                    sp.wait_ge(s_out, 32)


def lay_out(i):
    import numpy as np
    i = {k: np.asarray(v) for k, v in i.items()}
    src = np.full(EP, PAD, np.int32)
    dst = np.full(EP, PAD, np.int32)
    src[:E], dst[:E] = i["src"], i["dst"]
    a = {}
    a["x"] = np.zeros((NP, D), np.float32)
    a["x"][:N] = i["x"]
    a["src_cols"] = src.reshape(NCH, P).T
    a["dst_cols"] = dst.reshape(NCH, P).T
    a["dst"] = dst
    ext = np.concatenate([np.full(1, -1, np.int32), dst, np.full(1, NP, np.int32)])
    a["dst_ext"] = ext
    a["last"] = dst[P - 1::P]
    a["last_prev"] = np.concatenate([np.full(1, -1, np.int32), dst[P - 1::P][:-1]])
    rows = np.full((NCH + 1, P + 2), NP + 1, np.int32)
    rows[:NCH, 2:] = dst.reshape(NCH, P)
    rows[0, 0:2] = -1
    rows[1, 0] = -1
    rows[1:, 1] = dst[P - 1::P]
    rows[2:, 0] = dst[P - 1::P][:-1]
    a["dst_rows"] = rows
    srow = np.full((NCH + 1, P), PAD, np.int32)
    srow[:NCH] = src.reshape(NCH, P)
    a["src_rows"] = srow
    for n, k in ((16, "ea16T"), (64, "ea64T")):
        a[k] = np.zeros((n, EP), np.float32)
        a[k][:, :E] = i[f"edge_attr_{n}"].T
    a["L0_Wlr"] = np.concatenate([i["L0_gnn_W_l"], i["L0_gnn_W_r"]], 1)
    a["L0_blr"] = np.concatenate([i["L0_gnn_b_l"], i["L0_gnn_b_r"]])[None, :]
    a["L0_W_e"] = i["L0_gnn_W_e"]
    a["L0_att"] = i["L0_gnn_att"].reshape(D)
    for k in ("bias", "gamma", "beta"):
        a[f"L0_{k}"] = i[f"L0_gnn_{k}"]
    a["L1_W1T"] = i["L1_gnn_W1"].T
    a["L1_W2T2"] = np.concatenate([i["L1_gnn_W2"].T] * 2, 0)
    a["L1_W3T"] = i["L1_gnn_W3"].T
    a["L1_W4"] = i["L1_gnn_W4"]
    a["L2_MhT"] = i["L2_gnn_M_W"][:, :D].T
    a["L2_MxT"] = i["L2_gnn_M_W"][:, D:].T
    a["L2_Mb"] = i["L2_gnn_M_b"][None, :]
    a["L2_UT"] = i["L2_gnn_U_W"].T
    a["L2_Ub"] = i["L2_gnn_U_b"]
    a["L3_WT"] = i["L3_gnn_W"].T
    a["L3_b"] = i["L3_gnn_b"]
    return {k: np.ascontiguousarray(v) for k, v in a.items()}


def kernel(**inputs):
    import concourse.bacc as bacc
    from concourse.bass_utils import run_bass_kernel_spmd

    nc = bacc.Bacc("TRN2", target_bir_lowering=False, num_devices=1)
    arrays, d = {}, {}
    for name, a in lay_out(inputs).items():
        arrays[f"in_{name}"] = a
        d[name] = nc.dram_tensor(f"in_{name}", a.shape, mybir.dt.from_np(a.dtype), kind="ExternalInput").ap()
    out = nc.dram_tensor("out_x", (N, D), F32, kind="ExternalOutput").ap()
    gnn_kernel(nc, d, out)
    r = run_bass_kernel_spmd(nc, [arrays], core_ids=[0])
    return r.results[0]["out_x"]
```
